# Optimizing a Trainium2 kernel written in Bass

```python
import numpy as np
import jax
import jax.numpy as jnp

def _softmax(x, axis=-1):
    return jax.nn.softmax(x, axis=axis)

def _gelu(x):
    return jax.nn.gelu(x, approximate=True)

def _silu(x):
    return jax.nn.silu(x)

def _sigmoid(x):
    return jax.nn.sigmoid(x)

def _layernorm(x, axis=-1, eps=1e-05):
    m = jnp.mean(x, axis=axis, keepdims=True)
    v = jnp.var(x, axis=axis, keepdims=True)
    return (x - m) / jnp.sqrt(v + eps)

def _scatter_add(tgt, idx, src, axis=0):
    return tgt.at[idx].add(src)

def _segment_sum(src, seg, n):
    return jax.ops.segment_sum(src, seg, n)
kernel_name = 'mk_rec_standalone_d1_rec_r8_ec5f32'

def setup_inputs(seed: int=0):
    np.random.seed(seed)
    _w = jnp.asarray

    def _rec_inputs():
        import jax
        import jax.numpy as jnp
        _rk = jax.random.key(seed)
        r_x0 = jax.random.bernoulli(jax.random.fold_in(_rk, 1), 1e-05, (1024, 12500)).astype(jnp.float32)
        r_x1 = jax.random.bernoulli(jax.random.fold_in(_rk, 2), 2e-05, (1024, 6250)).astype(jnp.float32)
        r_x2 = jax.random.bernoulli(jax.random.fold_in(_rk, 3), 5e-05, (1024, 2500)).astype(jnp.float32)
        r_x3 = jax.random.bernoulli(jax.random.fold_in(_rk, 4), 0.0001, (1024, 1250)).astype(jnp.float32)
        r_x4 = jax.random.bernoulli(jax.random.fold_in(_rk, 5), 0.0002, (1024, 625)).astype(jnp.float32)
        r_x5 = jax.random.bernoulli(jax.random.fold_in(_rk, 6), 0.0005, (1024, 250)).astype(jnp.float32)
        r_x6 = jax.random.bernoulli(jax.random.fold_in(_rk, 7), 0.001, (1024, 1000)).astype(jnp.float32)
        r_x7 = jax.random.bernoulli(jax.random.fold_in(_rk, 8), 0.002, (1024, 500)).astype(jnp.float32)
        r_x8 = jax.random.bernoulli(jax.random.fold_in(_rk, 9), 0.005, (1024, 200)).astype(jnp.float32)
        r_x9 = jax.random.bernoulli(jax.random.fold_in(_rk, 10), 0.01, (1024, 100)).astype(jnp.float32)
        return (r_x0, r_x1, r_x2, r_x3, r_x4, r_x5, r_x6, r_x7, r_x8, r_x9)
    r_x0, r_x1, r_x2, r_x3, r_x4, r_x5, r_x6, r_x7, r_x8, r_x9 = _rec_inputs()

    def _L0_rec_setup():
        import jax, jax.numpy as jnp
        import numpy as np
        VOCABS = [12500, 6250, 2500, 1250, 625, 250, 1000, 500, 200, 100]
        BATCH = 1024
        EMB_DIM = 64
        key = jax.random.key(seed)
        inp = {}
        for i, v in enumerate(VOCABS):
            key, k_idx, k_w = jax.random.split(key, 3)
            idx = jax.random.randint(k_idx, (BATCH,), 0, v)
            inp[f'x{i}'] = jax.nn.one_hot(idx, v, dtype=jnp.float32)
            inp[f'w{i}'] = jax.random.normal(k_w, (v, EMB_DIM), dtype=jnp.float32) * 0.05
        return inp
    _L0_rec_all = _L0_rec_setup()
    _L0_rec_in = {k: v for k, v in _L0_rec_all.items() if k in ('w0', 'w1', 'w2', 'w3', 'w4', 'w5', 'w6', 'w7', 'w8', 'w9')}
    del _L0_rec_all
    return {'r_x0': r_x0, 'r_x1': r_x1, 'r_x2': r_x2, 'r_x3': r_x3, 'r_x4': r_x4, 'r_x5': r_x5, 'r_x6': r_x6, 'r_x7': r_x7, 'r_x8': r_x8, 'r_x9': r_x9, 'L0_rec_w0': _L0_rec_in['w0'], 'L0_rec_w1': _L0_rec_in['w1'], 'L0_rec_w2': _L0_rec_in['w2'], 'L0_rec_w3': _L0_rec_in['w3'], 'L0_rec_w4': _L0_rec_in['w4'], 'L0_rec_w5': _L0_rec_in['w5'], 'L0_rec_w6': _L0_rec_in['w6'], 'L0_rec_w7': _L0_rec_in['w7'], 'L0_rec_w8': _L0_rec_in['w8'], 'L0_rec_w9': _L0_rec_in['w9']}

def reference(r_x0, r_x1, r_x2, r_x3, r_x4, r_x5, r_x6, r_x7, r_x8, r_x9, L0_rec_w0, L0_rec_w1, L0_rec_w2, L0_rec_w3, L0_rec_w4, L0_rec_w5, L0_rec_w6, L0_rec_w7, L0_rec_w8, L0_rec_w9):
    import jax
    import jax.numpy as jnp

    def _L0_rec_ref(x0, x1, x2, x3, x4, x5, x6, x7, x8, x9, w0, w1, w2, w3, w4, w5, w6, w7, w8, w9):
        import jax, jax.numpy as jnp
        import numpy as np
        VOCABS = [12500, 6250, 2500, 1250, 625, 250, 1000, 500, 200, 100]
        BATCH = 1024
        EMB_DIM = 64
        xs = [x0, x1, x2, x3, x4, x5, x6, x7, x8, x9]
        ws = [w0, w1, w2, w3, w4, w5, w6, w7, w8, w9]
        embs = [jnp.dot(x, w) for x, w in zip(xs, ws)]
        emb_sum = embs[0]
        q_emb = jnp.dot(xs[0] ** 2, ws[0] ** 2)
        for i in range(1, len(xs)):
            emb_sum = emb_sum + embs[i]
            q_emb = q_emb + jnp.dot(xs[i] ** 2, ws[i] ** 2)
        fm_ans = 0.5 * (emb_sum ** 2 - q_emb)
        return jnp.concatenate([fm_ans] + embs, axis=-1)
    y = _L0_rec_ref(r_x0, r_x1, r_x2, r_x3, r_x4, r_x5, r_x6, r_x7, r_x8, r_x9, L0_rec_w0, L0_rec_w1, L0_rec_w2, L0_rec_w3, L0_rec_w4, L0_rec_w5, L0_rec_w6, L0_rec_w7, L0_rec_w8, L0_rec_w9)
    return y

_drawn_inputs = setup_inputs


def setup_inputs(seed=0):
    import zlib

    import numpy as np

    out = dict(_drawn_inputs(seed))
    spreads = {}
    factors = {}
    for name, (base, spread) in spreads.items():
        noise = np.random.default_rng([zlib.crc32(name.encode()), seed]).standard_normal(out[name].shape)
        drawn = base * np.exp(spread * noise) if base else spread * noise
        out[name] = jnp.asarray(drawn.astype(out[name].dtype))
    for name, factor in factors.items():
        out[name] = (out[name] * factor).astype(out[name].dtype)
    return out
```

```python
from contextlib import ExitStack

import concourse.bass as bass
from concourse import mybir

ALU = mybir.AluOpType
ACT = mybir.ActivationFunctionType
F32 = mybir.dt.float32
BF16 = mybir.dt.bfloat16
I32 = mybir.dt.int32

P = 128
D = 64
BATCH = 1024
NB = BATCH // P
PARTS = 6
PD = PARTS * D
VOCABS = [12500, 6250, 2500, 1250, 625, 250, 1000, 500, 200, 100]
NT = len(VOCABS)
TILES = [-(-v // P) for v in VOCABS]

ORDER = [
    (8, [[1, 1]]),
    (7, [[2, 2]]),
    (9, [[1]]),
    (6, [[4, 4]]),
    (5, [[2]]),
    (4, [[3, 2]]),
    (0, [[4, 3]] * 14),
    (1, [[4, 3]] * 7),
    (2, [[2, 2]] * 5),
    (3, [[4, 2], [3, 1]]),
]
SLOTS = 4
CHUNK = 4
GROUP = 8
NGROUPS = sum(len(groups) for _, groups in ORDER)
NCHUNKS = sum(len(g) for _, groups in ORDER for g in groups)


class Group:

    def __init__(self, table, index, chunk, tile, sizes):
        self.table, self.index, self.chunk, self.tile, self.sizes = table, index, chunk, tile, sizes
        self.tiles = sum(sizes)


def plan():
    tables, index, chunk = [], 0, 0
    for table, sizes in ORDER:
        groups, tile = [], 0
        for s in sizes:
            groups.append(Group(table, index, chunk, tile, s))
            index, chunk, tile = index + 1, chunk + len(s), tile + sum(s)
        assert tile == TILES[table]
        pairs = (len(groups) - 1) // 2
        looped = pairs > 1 and all(len(s) * 2 == SLOTS and s == sizes[0] for s in sizes)
        n = 2 * pairs if looped else 0
        tables.append((table, groups[0], groups[1:3] if looped else [], pairs if looped else 0,
                       groups[1 + n:], groups[-1]))
    return tables


def groups_in_order():
    index = chunk = 0
    for table, sizes in ORDER:
        for s in sizes:
            yield Group(table, index, chunk, 0, s)
            index, chunk = index + 1, chunk + len(s)


def rec_kernel(nc, xs, ws, out):
    tables = plan()
    chunks_before = [g.chunk for g in groups_in_order()]
    w_first = {}
    total = 0
    for t, _ in ORDER:
        w_first[t] = total
        total += TILES[t]

    x_dram = [x.rearrange("(p t) b -> p (t b)", p=P) for x in xs]
    w_dram = [w.rearrange("(p t) d -> p (t d)", p=P) for w in ws]

    with ExitStack() as ctx:
        def sb(name, shape, dt):
            return ctx.enter_context(nc.sbuf_tensor(name, shape, dt))

        def sem(name):
            return ctx.enter_context(nc.semaphore(name))

        sums = ctx.enter_context(nc.psum_tensor("sums", [P, NB, 512], F32))

        w_all = sb("w_all", [P, total * D], F32)
        x_ring = [sb(f"x_ring{s}", [P, CHUNK * BATCH], F32) for s in range(SLOTS)]
        parts = [sb(f"parts{i}", [P, GROUP, PD], BF16) for i in range(2)]
        w_now = sb("w_now", [P, GROUP, D], F32)
        w_rest = sb("w_rest", [P, GROUP, D], F32)
        w_square = sb("w_square", [P, GROUP, D], F32)
        q_rest = sb("q_rest", [P, GROUP, D], F32)
        differs = [sb(f"differs{i}", [P, CHUNK * BATCH], BF16) for i in range(2)]
        odd_counts = sb("odd_counts", [P, NCHUNKS], F32)
        odd_total = sb("odd_total", [P, 1], F32)
        odd_flag = sb("odd_flag", [1, 1], I32)
        ones = sb("ones", [P, 1], F32)
        zeros = sb("zeros", [P, P], BF16)
        stage = sb("stage", [P, NB, PD], F32)
        low_sum = sb("low_sum", [P, NB, D], F32)
        emb_sum = sb("emb_sum", [P, NB, D], F32)
        q_sum = sb("q_sum", [P, NB, 3 * D], F32)
        out_sb = sb("out_sb", [P, NT + 1, NB, D], F32)

        w_landed = [sem(f"w_landed{t}") for t in range(NT)]
        x_landed = [sem(f"x_landed{s}") for s in range(SLOTS)]
        x_multiplied = sem("x_multiplied")
        x_checked = sem("x_checked")
        w_copied = sem("w_copied")
        w_high = sem("w_high")
        w_middle = sem("w_middle")
        w_rested = sem("w_rested")
        squared = sem("squared")
        q_high = sem("q_high")
        q_middle = sem("q_middle")
        q_rested = sem("q_rested")
        w_low = sem("w_low")
        parts_ready = sem("parts_ready")
        constants = sem("constants")
        bank_copied = sem("bank_copied")
        combined = sem("combined")
        table_out = sem("table_out")
        stage_used = sem("stage_used")
        odd_ready = sem("odd_ready")
        odd_summed = sem("odd_summed")
        flag_ready = sem("flag_ready")
        stored = sem("stored")

        gx_landed = sem("gx_landed")
        gx_ready = sem("gx_ready")
        g_multiplied = sem("g_multiplied")
        g_added = sem("g_added")
        g_chain = sem("g_chain")
        g_done = sem("g_done")

        block = ctx.enter_context(nc.Block())

        def run(eng, table, step, between=None):
            _, head, pair, pairs, rest, _ = table
            step(head, 0, head.chunk, head.index)
            if between:
                between()
            if pairs:
                with eng.Fori(0, pairs) as i:
                    for group in pair:
                        step(group, i, group.chunk + SLOTS * i, group.index + 2 * i)
            for group in rest:
                step(group, 0, group.chunk, group.index)

        def w_tiles(group, i):
            at = (w_first[group.table] + group.tile + 2 * group.tiles * i) * D
            return w_all[:, bass.ds(at, group.tiles * D)].rearrange("p (t d) -> p t d", d=D)

        @block.sync
        def _(sp):
            def load(group, i, k, g):
                at = group.tile + 2 * group.tiles * i
                for c, n in enumerate(group.sizes):
                    slot = (group.chunk + c) % SLOTS
                    if group.chunk + c >= SLOTS:
                        sp.wait_ge(x_multiplied, k + (c + 1 - SLOTS))
                        sp.wait_ge(x_checked, k + (c + 1 - SLOTS))
                    sp.dma_start(x_ring[slot][:, 0:n * BATCH],
                                 x_dram[group.table][:, bass.ds(at * BATCH, n * BATCH)]
                                 ).then_inc(x_landed[slot], 16)
                    at = at + n

            for table in tables:
                run(sp, table, load)
            for n, (t, _) in enumerate(ORDER):
                sp.wait_ge(table_out, n + 1)
                sp.dma_start(out[t + 1], out_sb[:, t + 1, :, :]).then_inc(stored, 16)
            sp.wait_ge(table_out, NT + 1)
            sp.dma_start(out[0], out_sb[:, 0, :, :]).then_inc(stored, 16)
            sp.wait_ge(stored, 16 * (NT + 1))

            sp.wait_ge(flag_ready, 1)
            odd = sp.value_load(odd_flag[0:1, 0:1], min_val=0, max_val=1)
            with sp.If(odd != 0):
                for n, (t, _) in enumerate(ORDER):
                    base = w_first[t]
                    with sp.Fori(0, TILES[t]) as i:
                        sp.wait_ge(g_multiplied, base + i + 1)
                        sp.dma_start(x_ring[0][:, 0:BATCH],
                                     x_dram[t][:, bass.ds(i * BATCH, BATCH)]).then_inc(gx_landed, 16)
                sp.wait_ge(g_done, 1)
                for t in range(NT + 1):
                    sp.dma_start(out[t], out_sb[:, t, :, :]).then_inc(stored, 16)
                sp.wait_ge(stored, 2 * 16 * (NT + 1))

        @block.scalar
        def _(act):
            for t, _ in ORDER:
                act.dma_start(w_all[:, w_first[t] * D:(w_first[t] + TILES[t]) * D],
                              w_dram[t]).then_inc(w_landed[t], 16)

            def split(group, i, k, g):
                part = parts[group.index % 2][:, 0:group.tiles, :]
                if group.index >= 2:
                    act.wait_ge(x_multiplied, k - (group.chunk - chunks_before[group.index - 1]))
                act.wait_ge(w_copied, g + 1)
                nc.scalar.activation(part[:, :, 0:D], w_now[:, 0:group.tiles, :], ACT.Copy).then_inc(w_high, 1)
                act.wait_ge(squared, g + 1)
                nc.scalar.activation(part[:, :, 3 * D:4 * D], w_square[:, 0:group.tiles, :],
                                     ACT.Copy).then_inc(q_high, 1)
                act.wait_ge(w_rested, g + 1)
                nc.scalar.activation(part[:, :, D:2 * D], w_rest[:, 0:group.tiles, :],
                                     ACT.Copy).then_inc(w_middle, 1)
                act.wait_ge(q_rested, g + 1)
                nc.scalar.activation(part[:, :, 4 * D:5 * D], q_rest[:, 0:group.tiles, :],
                                     ACT.Copy).then_inc(q_middle, 1)

            def to_stage(n):
                last = tables[n][5]
                if n:
                    act.wait_ge(stage_used, n)
                act.wait_ge(x_multiplied, last.chunk + len(last.sizes))
                for b in range(NB):
                    nc.scalar.activation(stage[:, b, :], sums[:, b, 0:PD], ACT.Copy
                                         ).then_inc(bank_copied, 1)

            for n, table in enumerate(tables):
                run(act, table, split, (lambda m=n - 1: to_stage(m)) if n else None)
            to_stage(NT - 1)

        @block.gpsimd
        def _(pool):
            def split(group, i, k, g):
                part = parts[group.index % 2][:, 0:group.tiles, :]
                w = w_now[:, 0:group.tiles, :]
                rest, square = w_rest[:, 0:group.tiles, :], w_square[:, 0:group.tiles, :]
                qrest = q_rest[:, 0:group.tiles, :]
                if group.index:
                    pool.wait_ge(parts_ready, g)
                pool.wait_ge(w_landed[group.table], 16)
                nc.gpsimd.tensor_copy(w, w_tiles(group, i)).then_inc(w_copied, 1)
                pool.wait_ge(w_copied, g + 1)
                nc.gpsimd.tensor_tensor(square, w, w, ALU.mult).then_inc(squared, 1)
                pool.wait_ge(w_high, g + 1)
                nc.gpsimd.tensor_tensor(rest, w, part[:, :, 0:D], ALU.subtract).then_inc(w_rested, 1)
                pool.wait_ge(q_high, g + 1)
                nc.gpsimd.tensor_tensor(qrest, square, part[:, :, 3 * D:4 * D], ALU.subtract
                                        ).then_inc(q_rested, 1)
                pool.wait_ge(w_middle, g + 1)
                nc.gpsimd.tensor_tensor(part[:, :, 2 * D:3 * D], rest, part[:, :, D:2 * D],
                                        ALU.subtract).then_inc(w_low, 1)
                pool.wait_ge(q_middle, g + 1)
                nc.gpsimd.tensor_tensor(part[:, :, 5 * D:6 * D], qrest, part[:, :, 4 * D:5 * D],
                                        ALU.subtract).then_inc(parts_ready, 1)

            for table in tables:
                run(pool, table, split)

        @block.tensor
        def _(pe):
            def multiply(group, i, k, g):
                part = parts[group.index % 2]
                pe.wait_ge(w_low, g + 1)
                pe.wait_ge(parts_ready, g + 1)
                tile = 0
                for c, n in enumerate(group.sizes):
                    slot = (group.chunk + c) % SLOTS
                    pe.wait_ge(x_landed[slot], 16 * ((group.chunk + c) // SLOTS + 1 + i))
                    x = x_ring[slot][:, :].bitcast(BF16).rearrange("p (t b h) -> p t b h", h=2, b=BATCH)
                    for t in range(n):
                        for b in range(NB):
                            last = nc.tensor.matmul(sums[:, b, 0:PD], x[:, t, b * P:(b + 1) * P, 1],
                                                    part[:, tile, :], start=False, stop=False,
                                                    skip_group_check=True)
                        tile += 1
                    last.then_inc(x_multiplied, 1)

            pe.wait_ge(constants, 1)
            for n, table in enumerate(tables):
                for b in range(NB):
                    if n:
                        pe.wait_ge(bank_copied, NB * (n - 1) + b + 1)
                    nc.tensor.matmul(sums[:, b, PD:PD + 1], zeros[:, :], zeros[:, 0:1],
                                     start=True, stop=True, skip_group_check=True)
                run(pe, table, multiply)

            pe.wait_ge(constants, 2)
            pe.wait_ge(bank_copied, NB * (NT - 1) + 1)
            pe.wait_ge(odd_ready, 1)
            nc.tensor.matmul(sums[0:1, 0, PD:PD + 1], odd_total[:, :], ones[:, :], start=True,
                             stop=True, skip_group_check=True).then_inc(odd_summed, 1)
            pe.wait_ge(flag_ready, 1)
            odd = pe.value_load(odd_flag[0:1, 0:1], min_val=0, max_val=1)
            with pe.If(odd != 0):
                w_tile, wq_tile = w_rest[:, 0, :], w_square[:, 0, :]
                for t, _ in ORDER:
                    base = w_first[t]
                    with pe.Fori(0, TILES[t]) as i:
                        pe.wait_ge(gx_landed, 16 * (base + i + 1))
                        pe.wait_ge(gx_ready, base + i + 1)
                        for b in range(NB):
                            nc.tensor.matmul(sums[:, b, 0:D], x_ring[0][:, b * P:(b + 1) * P],
                                             w_tile, start=True, stop=True, skip_group_check=True)
                            last = nc.tensor.matmul(sums[:, b, D:2 * D], x_ring[1][:, b * P:(b + 1) * P],
                                                    wq_tile, start=False, stop=True,
                                                    skip_group_check=True)
                        last.then_inc(g_multiplied, 1)

        @block.vector
        def _(dve):
            nc.vector.memset(zeros[:, :], 0.0).then_inc(constants, 1)
            nc.vector.memset(ones[:, :], 1.0).then_inc(constants, 1)
            nc.vector.memset(emb_sum[:, :, :], 0.0).then_inc(constants, 1)
            nc.vector.memset(q_sum[:, :, :], 0.0).then_inc(constants, 1)

            def check(group, i, k, g):
                for c, n in enumerate(group.sizes):
                    slot = (group.chunk + c) % SLOTS
                    dve.wait_ge(x_landed[slot], 16 * ((group.chunk + c) // SLOTS + 1 + i))
                    if group.chunk + c >= 2:
                        dve.wait_ge(x_checked, k + c - 1)
                    x = x_ring[slot][:, 0:n * BATCH]
                    nc.vector.scalar_tensor_tensor(out=differs[(group.chunk + c) % 2][:, 0:n * BATCH], in0=x, scalar=0.0,
                                                   in1=x, op0=ALU.is_gt, op1=ALU.not_equal,
                                                   accum_out=odd_counts[:, bass.ds(k + c, 1)]
                                                   ).then_inc(x_checked, 1)

            chain = [0]

            def link(ins, done):
                ins.then_inc(done, 1)
                chain[0] += 1
                dve.wait_ge(done, chain[0])

            def combine(n):
                t = ORDER[n][0]
                emb = out_sb[:, t + 1, :, :]
                if n == 0:
                    dve.wait_ge(constants, 4)
                dve.wait_ge(bank_copied, NB * (n + 1))
                link(nc.vector.tensor_tensor(low_sum[:, :, :], stage[:, :, D:2 * D],
                                             stage[:, :, 2 * D:3 * D], ALU.add), combined)
                link(nc.vector.tensor_tensor(emb, low_sum[:, :, :], stage[:, :, 0:D], ALU.add), combined)
                link(nc.vector.tensor_tensor(q_sum[:, :, :], q_sum[:, :, :], stage[:, :, 3 * D:6 * D],
                                             ALU.add), combined)
                nc.vector.tensor_tensor(emb_sum[:, :, :], emb_sum[:, :, :], emb, ALU.add
                                        ).then_inc(stage_used, 1)
                dve.wait_ge(stage_used, n + 1)
                nc.vector.nop().then_inc(table_out, 1)

            for n, table in enumerate(tables):
                run(dve, table, check, (lambda m=n - 1: combine(m)) if n else None)
            dve.wait_ge(x_checked, NCHUNKS)
            nc.vector.tensor_reduce(odd_total[:, :], odd_counts[:, :], mybir.AxisListType.X,
                                    ALU.add).then_inc(odd_ready, 1)
            combine(NT - 1)
            fm = out_sb[:, 0, :, :]
            link(nc.vector.tensor_tensor(low_sum[:, :, :], q_sum[:, :, D:2 * D],
                                         q_sum[:, :, 2 * D:3 * D], ALU.add), combined)
            link(nc.vector.tensor_tensor(low_sum[:, :, :], low_sum[:, :, :], q_sum[:, :, 0:D],
                                         ALU.add), combined)
            link(nc.vector.tensor_tensor(fm, emb_sum[:, :, :], emb_sum[:, :, :], ALU.mult), combined)
            link(nc.vector.tensor_tensor(fm, fm, low_sum[:, :, :], ALU.subtract), combined)
            nc.vector.tensor_scalar(fm, fm, 0.5, None, ALU.mult).then_inc(table_out, 1)
            dve.wait_ge(odd_summed, 1)
            nc.vector.tensor_scalar(odd_flag[0:1, 0:1], sums[0:1, 0, PD:PD + 1], 1.0, None,
                                    ALU.min).then_inc(flag_ready, 1)
            dve.wait_ge(flag_ready, 1)
            odd = dve.value_load(odd_flag[0:1, 0:1], min_val=0, max_val=1)
            with dve.If(odd != 0):
                steps = [0]

                def g_link(ins):
                    ins.then_inc(g_chain, 1)
                    steps[0] += 1
                    dve.wait_ge(g_chain, steps[0])

                q = q_sum[:, :, 0:D]
                dve.wait_ge(stored, 16 * (NT + 1))
                dve.wait_ge(x_multiplied, NCHUNKS)
                dve.wait_ge(parts_ready, NGROUPS)
                nc.vector.nop().then_inc(g_multiplied, 1)
                g_link(nc.vector.memset(q_sum[:, :, :], 0.0))
                g_link(nc.vector.memset(emb_sum[:, :, :], 0.0))
                for t, _ in ORDER:
                    base = w_first[t]
                    emb = out_sb[:, t + 1, :, :]
                    g_link(nc.vector.memset(emb, 0.0))
                    with dve.Fori(0, TILES[t]) as i:
                        dve.wait_ge(gx_landed, 16 * (base + i + 1))
                        w = w_all[:, bass.ds((base + i) * D, D)]
                        nc.vector.tensor_tensor(x_ring[1][:, 0:BATCH], x_ring[0][:, 0:BATCH],
                                                x_ring[0][:, 0:BATCH], ALU.mult)
                        nc.vector.tensor_tensor(w_square[:, 0, :], w, w, ALU.mult)
                        nc.vector.tensor_copy(w_rest[:, 0, :], w).then_inc(gx_ready, 1)
                        dve.wait_ge(g_multiplied, base + i + 2)
                        nc.vector.tensor_tensor(emb, emb, sums[:, :, 0:D], ALU.add)
                        nc.vector.tensor_tensor(q, q, sums[:, :, D:2 * D], ALU.add).then_inc(g_added, 1)
                        dve.wait_ge(g_added, base + i + 1)
                    g_link(nc.vector.tensor_tensor(emb_sum[:, :, :], emb_sum[:, :, :], emb, ALU.add))
                g_link(nc.vector.tensor_tensor(fm, emb_sum[:, :, :], emb_sum[:, :, :], ALU.mult))
                g_link(nc.vector.tensor_tensor(fm, fm, q, ALU.subtract))
                nc.vector.tensor_scalar(fm, fm, 0.5, None, ALU.mult).then_inc(g_done, 1)


def kernel(**inputs):
    import numpy as _np
    import concourse.bacc as _bacc
    from concourse.bass_utils import run_bass_kernel_spmd as _run

    nc = _bacc.Bacc("TRN2", target_bir_lowering=False, num_devices=1)
    arrays, xs, ws = {}, [], []
    for i, tiles in enumerate(TILES):
        x, w = _np.asarray(inputs[f"r_x{i}"]), _np.asarray(inputs[f"L0_rec_w{i}"])
        pad = ((0, tiles * P - VOCABS[i]), (0, 0))
        for name, a, aps in ((f"in_x{i}_dram", x.T, xs), (f"in_w{i}_dram", w, ws)):
            a = _np.ascontiguousarray(_np.pad(a, pad))
            arrays[name] = a
            aps.append(nc.dram_tensor(name, a.shape, F32, kind="ExternalInput").ap())
    out = nc.dram_tensor("out_0_dram", (NT + 1, P, NB, D), F32, kind="ExternalOutput").ap()
    rec_kernel(nc, xs, ws, out)
    r = _run(nc, [arrays], core_ids=[0])
    got = r.results[0]["out_0_dram"]
    return _np.ascontiguousarray(got.transpose(2, 1, 0, 3).reshape(BATCH, (NT + 1) * D))
```

```python
from contextlib import ExitStack

import concourse.bass as bass
from concourse import mybir

ALU = mybir.AluOpType
ACT = mybir.ActivationFunctionType
F32 = mybir.dt.float32
BF16 = mybir.dt.bfloat16
I32 = mybir.dt.int32

P = 128
D = 64
BATCH = 1024
NB = BATCH // P
PARTS = 6
PD = PARTS * D
VOCABS = [12500, 6250, 2500, 1250, 625, 250, 1000, 500, 200, 100]
NT = len(VOCABS)
TILES = [-(-v // P) for v in VOCABS]

FULL = [2, 2, 2, 2]
ORDER = [
    (8, [[1, 1]]),
    (6, [FULL]),
    (7, [[2, 2]]),
    (4, [[2, 2, 1]]),
    (0, [FULL] * 11 + [[2, 2, 1]] * 2),
    (9, [[1]]),
    (5, [[2]]),
    (1, [FULL] * 5 + [[2, 2], [2, 2, 1]]),
    (3, [[2, 2, 2], [2, 2]]),
    (2, [FULL, [2, 2, 2], [2, 2, 1, 1]]),
]

STEPS = [
    ("load", 8), ("load", 6), ("load", 7), ("load", 4), ("load", 0),
    ("head", 8), ("head", 6), ("stage", 8), ("head", 7), ("stage", 6), ("head", 4), ("stage", 7),
    ("head", 0), ("stage", 4), ("load", 9), ("load", 5), ("load", 1),
    ("rest", 0), ("load", 3), ("load", 2), ("head", 9), ("head", 5), ("head", 1), ("stage", 0), ("stage", 9), ("stage", 5),
    ("rest", 1), ("head", 3), ("stage", 1), ("rest", 3), ("head", 2), ("stage", 3), ("rest", 2),
]
IN_ROOM_OF_0 = (2, 3)
SLOTS = 2 * len(FULL)
CHUNK = max(FULL)
GROUP = sum(FULL)
NGROUPS = sum(len(groups) for _, groups in ORDER)
NCHUNKS = sum(len(g) for _, groups in ORDER for g in groups)


class Group:

    def __init__(self, table, chunk, tile, sizes):
        self.table, self.chunk, self.tile, self.sizes = table, chunk, tile, sizes
        self.tiles = sum(sizes)
        self.last = False
        self.split = self.buffer = self.free_after = None


class Table:

    def __init__(self, table, sizes, chunk):
        self.table, self.groups, tile = table, [], 0
        for s in sizes:
            self.groups.append(Group(table, chunk, tile, s))
            chunk, tile = chunk + len(s), tile + sum(s)
        assert tile == TILES[table]
        self.groups[-1].last = True
        self.end = chunk
        pairs = (sizes.count(FULL) - 1) // 2
        self.pairs = pairs if pairs > 1 else 0
        assert all(s == FULL for s in sizes[:1 + 2 * self.pairs]) or not self.pairs
        self.looped = self.groups[1:3] if self.pairs else []
        self.straight = self.groups[1 + 2 * self.pairs:]


def plan():
    tables, chunk = {}, 0
    for t, sizes in ORDER:
        tables[t] = Table(t, sizes, chunk)
        chunk = tables[t].end
    split, shared = 0, []
    for step, t in STEPS:
        if step not in ("head", "rest"):
            continue
        for group in tables[t].groups[:1] if step == "head" else tables[t].groups[1:]:
            group.split, split = split, split + 1
            if len(tables[t].groups) == 1:
                group.buffer = f"parts_of_{t}"
                continue
            group.buffer = f"parts{len(shared) % 2}"
            if group in tables[t].looped:
                group.free_after = group.chunk - len(group.sizes)
            elif len(shared) >= 2:
                group.free_after = shared[-2].chunk + len(shared[-2].sizes)
            shared.append(group)
    return tables


def rec_kernel(nc, xs, ws, out):
    tables = plan()
    w_first = {}
    total = 0
    for t, _ in ORDER:
        if t not in IN_ROOM_OF_0:
            w_first[t] = total
            total += TILES[t]
    at = w_first[0]
    for t in IN_ROOM_OF_0:
        w_first[t] = at
        at += TILES[t]
    assert at <= w_first[0] + TILES[0]

    x_dram = [x.rearrange("(p t) b -> p (t b)", p=P) for x in xs]
    w_dram = [w.rearrange("(p t) d -> p (t d)", p=P) for w in ws]

    with ExitStack() as ctx:
        def sb(name, shape, dt):
            return ctx.enter_context(nc.sbuf_tensor(name, shape, dt))

        def sem(name):
            return ctx.enter_context(nc.semaphore(name))

        sums = ctx.enter_context(nc.psum_tensor("sums", [P, NB, 512], F32))

        w_all = sb("w_all", [P, total * D], F32)
        x_ring = [sb(f"x_ring{s}", [P, CHUNK * BATCH], F32) for s in range(SLOTS)]
        parts = {f"parts{i}": sb(f"parts{i}", [P, GROUP, PD], BF16) for i in range(2)}
        for t, table in tables.items():
            if len(table.groups) == 1:
                name = table.groups[0].buffer
                parts[name] = sb(name, [P, TILES[t], PD], BF16)
        w_now = sb("w_now", [P, GROUP, D], F32)
        w_rest = sb("w_rest", [P, GROUP, D], F32)
        w_square = sb("w_square", [P, GROUP, D], F32)
        q_rest = sb("q_rest", [P, GROUP, D], F32)
        differs = [sb(f"differs{i}", [P, CHUNK * BATCH], mybir.dt.uint8) for i in range(2)]
        odd_counts = sb("odd_counts", [P, NCHUNKS], F32)
        odd_total = sb("odd_total", [P, 1], F32)
        odd_flag = sb("odd_flag", [1, 1], I32)
        ones = sb("ones", [P, 1], F32)
        zeros = sb("zeros", [P, P], BF16)
        stages = [sb(f"stage{i}", [P, NB, PD], F32) for i in range(2)]
        low_sum = sb("low_sum", [P, NB, D], F32)
        emb_sum = sb("emb_sum", [P, NB, D], F32)
        q_low = sb("q_low", [P, NB, D], F32)[:, :, :]
        q_total = sb("q_total", [P, NB, D], F32)
        q_last = sb("q_last", [P, NB, D], F32)
        out_sb = sb("out_sb", [P, NT + 1, NB, D], F32)

        w_landed = [sem(f"w_landed{t}") for t in range(NT)]
        x_landed = [sem(f"x_landed{s}") for s in range(SLOTS)]
        x_multiplied = sem("x_multiplied")
        x_checked = sem("x_checked")
        w_copied = sem("w_copied")
        w_high = sem("w_high")
        w_middle = sem("w_middle")
        w_rested = sem("w_rested")
        squared = sem("squared")
        q_high = sem("q_high")
        q_middle = sem("q_middle")
        q_rested = sem("q_rested")
        w_low = sem("w_low")
        parts_ready = sem("parts_ready")
        constants = sem("constants")
        bank_summed = sem("bank_summed")
        even_copied = sem("even_copied")
        odd_copied = sem("odd_copied")
        combined = sem("combined")
        fm_ready = sem("fm_ready")
        last_emb = sem("last_emb")
        last_q_copied = sem("last_q_copied")
        last_q_summed = sem("last_q_summed")
        q_chain = sem("q_chain")
        emb_added = sem("emb_added")
        q_added = sem("q_added")
        odd_ready = sem("odd_ready")
        odd_summed = sem("odd_summed")
        flag_ready = sem("flag_ready")
        stored = sem("stored")

        gx_landed = sem("gx_landed")
        gw_landed = sem("gw_landed")
        gx_ready = sem("gx_ready")
        g_multiplied = sem("g_multiplied")
        g_added = sem("g_added")
        g_chain = sem("g_chain")
        g_done = sem("g_done")

        block = ctx.enter_context(nc.Block())

        last_stage = stages[(NT - 1) % 2]
        lower, upper = slice(0, NB // 2), slice(NB // 2, NB)

        def run_head(eng, table, step):
            group = table.groups[0]
            step(group, 0, group.chunk, group.split)

        def run_rest(eng, table, step):
            if table.pairs:
                with eng.Fori(0, table.pairs) as i:
                    for group in table.looped:
                        step(group, i, group.chunk + SLOTS * i, group.split + 2 * i)
            for group in table.straight:
                step(group, 0, group.chunk, group.split)

        def wait_whole(eng, n, b):
            if b < NB - 1:
                eng.wait_ge(bank_summed, (NB - 1) * n + b + 1)
            else:
                eng.wait_ge(x_multiplied, tables[ORDER[n][0]].end)

        def w_tiles(group, i):
            at = (w_first[group.table] + group.tile + 2 * group.tiles * i) * D
            return w_all[:, bass.ds(at, group.tiles * D)].rearrange("p (t d) -> p t d", d=D)

        @block.sync
        def _(sp):
            def load(group, i, k, g):
                at = group.tile + 2 * group.tiles * i
                for c, n in enumerate(group.sizes):
                    slot = (group.chunk + c) % SLOTS
                    if group.chunk + c >= SLOTS:
                        sp.wait_ge(x_multiplied, k + (c + 1 - SLOTS))
                        sp.wait_ge(x_checked, k + (c + 1 - SLOTS))
                    sp.dma_start(x_ring[slot][:, 0:n * BATCH],
                                 x_dram[group.table][:, bass.ds(at * BATCH, n * BATCH)]
                                 ).then_inc(x_landed[slot], 16)
                    at = at + n

            for t, _ in ORDER:
                run_head(sp, tables[t], load)
                run_rest(sp, tables[t], load)
            sp.wait_ge(last_emb, 2)
            sp.dma_start(out[ORDER[-1][0] + 1], out_sb[:, ORDER[-1][0] + 1, :, :]).then_inc(stored, 16)
            sp.wait_ge(fm_ready, 1)
            sp.dma_start(out[0], out_sb[:, 0, :, :]).then_inc(stored, 16)
            sp.wait_ge(flag_ready, 1)
            odd = sp.value_load(odd_flag[0:1, 0:1], min_val=0, max_val=P * NCHUNKS * CHUNK * BATCH)
            sp.wait_ge(stored, 16 * (NT + 1))
            with sp.If(odd != 0):
                for t in range(NT):
                    base = sum(TILES[:t])
                    with sp.Fori(0, TILES[t]) as i:
                        sp.wait_ge(g_multiplied, base + i + 1)
                        sp.dma_start(x_ring[0][:, 0:BATCH],
                                     x_dram[t][:, bass.ds(i * BATCH, BATCH)]).then_inc(gx_landed, 16)
                        sp.dma_start(w_rest[:, 0, :], w_dram[t][:, bass.ds(i * D, D)]
                                     ).then_inc(gw_landed, 16)
                sp.wait_ge(g_done, 1)
                for t in range(NT + 1):
                    sp.dma_start(out[t], out_sb[:, t, :, :]).then_inc(stored, 16)
                sp.wait_ge(stored, 2 * 16 * (NT + 1))

        @block.scalar
        def _(act):
            def load(t):
                if t in IN_ROOM_OF_0:
                    act.wait_ge(w_copied, tables[0].groups[-1].split + 1)
                act.dma_start(w_all[:, w_first[t] * D:(w_first[t] + TILES[t]) * D],
                              w_dram[t]).then_inc(w_landed[t], 16)

            def split(group, i, k, g):
                part = parts[group.buffer][:, 0:group.tiles, :]
                if group.free_after is not None:
                    act.wait_ge(x_multiplied, k - (group.chunk - group.free_after))
                act.wait_ge(w_copied, g + 1)
                nc.scalar.activation(part[:, :, 0:D], w_now[:, 0:group.tiles, :], ACT.Copy).then_inc(w_high, 1)
                act.wait_ge(squared, g + 1)
                nc.scalar.activation(part[:, :, 3 * D:4 * D], w_square[:, 0:group.tiles, :],
                                     ACT.Copy).then_inc(q_high, 1)
                act.wait_ge(w_rested, g + 1)
                nc.scalar.activation(part[:, :, D:2 * D], w_rest[:, 0:group.tiles, :],
                                     ACT.Copy).then_inc(w_middle, 1)
                act.wait_ge(q_rested, g + 1)
                nc.scalar.activation(part[:, :, 4 * D:5 * D], q_rest[:, 0:group.tiles, :],
                                     ACT.Copy).then_inc(q_middle, 1)

            def store(n):
                t = ORDER[n][0]
                act.dma_start(out[t + 1], out_sb[:, t + 1, :, :]).then_inc(stored, 16)

            def to_stage(n):
                stage = stages[n % 2]
                if n >= 2:
                    act.wait_ge(emb_added, n - 1)
                    act.wait_ge(q_added, n - 1)
                    store(n - 2)
                for b in range(0, NB, 2):
                    wait_whole(act, n, b)
                    nc.scalar.activation(stage[:, b, :], sums[:, b, 0:PD], ACT.Copy
                                         ).then_inc(even_copied, 1)

            for step, t in STEPS:
                if step == "load":
                    load(t)
                elif step == "head":
                    run_head(act, tables[t], split)
                elif step == "rest":
                    run_rest(act, tables[t], split)
                else:
                    to_stage([u for u, _ in ORDER].index(t))

            for n in range(NT - 3, NT - 1):
                act.wait_ge(emb_added, n + 1)
                store(n)
            for step, banks in enumerate((upper, lower)):
                if step:
                    act.wait_ge(last_emb, 1)
                else:
                    wait_whole(act, NT - 1, NB - 1)
                nc.scalar.activation(last_stage[:, banks, 3 * D:], sums[:, banks, 3 * D:PD],
                                     ACT.Copy).then_inc(last_q_copied, 1)
            act.wait_ge(odd_summed, 1)
            nc.scalar.activation(odd_flag[0:1, 0:1], sums[0:1, NB - 1, PD:PD + 1], ACT.Copy
                                 ).then_inc(flag_ready, 1)

        @block.gpsimd
        def _(pool):
            def split(group, i, k, g):
                part = parts[group.buffer][:, 0:group.tiles, :]
                w = w_now[:, 0:group.tiles, :]
                rest, square = w_rest[:, 0:group.tiles, :], w_square[:, 0:group.tiles, :]
                qrest = q_rest[:, 0:group.tiles, :]
                if group.split:
                    pool.wait_ge(parts_ready, g)
                pool.wait_ge(w_landed[group.table], 16)
                nc.gpsimd.tensor_copy(w, w_tiles(group, i)).then_inc(w_copied, 1)
                pool.wait_ge(w_copied, g + 1)
                nc.gpsimd.tensor_tensor(square, w, w, ALU.mult).then_inc(squared, 1)
                pool.wait_ge(w_high, g + 1)
                nc.gpsimd.tensor_tensor(rest, w, part[:, :, 0:D], ALU.subtract).then_inc(w_rested, 1)
                pool.wait_ge(q_high, g + 1)
                nc.gpsimd.tensor_tensor(qrest, square, part[:, :, 3 * D:4 * D], ALU.subtract
                                        ).then_inc(q_rested, 1)
                pool.wait_ge(w_middle, g + 1)
                nc.gpsimd.tensor_tensor(part[:, :, 2 * D:3 * D], rest, part[:, :, D:2 * D],
                                        ALU.subtract).then_inc(w_low, 1)
                pool.wait_ge(q_middle, g + 1)
                nc.gpsimd.tensor_tensor(part[:, :, 5 * D:6 * D], qrest, part[:, :, 4 * D:5 * D],
                                        ALU.subtract).then_inc(parts_ready, 1)

            def combine_q(n):
                stage = stages[n % 2]
                pool.wait_ge(even_copied, NB // 2 * (n + 1))
                pool.wait_ge(odd_copied, NB // 2 * (n + 1))
                nc.gpsimd.tensor_tensor(q_low, stage[:, :, 4 * D:5 * D], stage[:, :, 5 * D:], ALU.add
                                        ).then_inc(q_chain, 1)
                pool.wait_ge(q_chain, 2 * n + 1)
                nc.gpsimd.tensor_tensor(q_last[:, :, :], q_low, stage[:, :, 3 * D:4 * D], ALU.add
                                        ).then_inc(q_chain, 1)
                pool.wait_ge(q_chain, 2 * n + 2)
                if n == 0:
                    pool.wait_ge(constants, 4)
                nc.gpsimd.tensor_tensor(q_total[:, :, :], q_total[:, :, :], q_last[:, :, :], ALU.add
                                        ).then_inc(q_added, 1)
                pool.wait_ge(q_added, n + 1)

            for step, t in STEPS:
                if step == "head":
                    run_head(pool, tables[t], split)
                elif step == "rest":
                    run_rest(pool, tables[t], split)
                elif step == "stage":
                    combine_q([u for u, _ in ORDER].index(t))

            for step, banks in enumerate((upper, lower)):
                q, part = q_last[:, banks, :], last_stage[:, banks, :]
                pool.wait_ge(last_q_copied, step + 1)
                nc.gpsimd.tensor_tensor(q, part[:, :, 4 * D:5 * D], part[:, :, 5 * D:], ALU.add
                                        ).then_inc(q_chain, 1)
                pool.wait_ge(q_chain, 2 * (NT - 1) + step + 1)
                nc.gpsimd.tensor_tensor(q, q, part[:, :, 3 * D:4 * D], ALU.add
                                        ).then_inc(last_q_summed, 1)

        @block.tensor
        def _(pe):
            def multiply(group, i, k, g):
                part = parts[group.buffer]
                pe.wait_ge(w_low, g + 1)
                pe.wait_ge(parts_ready, g + 1)
                tile = 0
                for c, n in enumerate(group.sizes):
                    slot = (group.chunk + c) % SLOTS
                    pe.wait_ge(x_landed[slot], 16 * ((group.chunk + c) // SLOTS + 1 + i))
                    x = x_ring[slot][:, :].bitcast(BF16).rearrange("p (t b h) -> p t b h", h=2, b=BATCH)
                    for t in range(n):
                        tile += 1
                        whole = group.last and tile == group.tiles
                        for b in range(NB):
                            last = nc.tensor.matmul(sums[:, b, 0:PD], x[:, t, b * P:(b + 1) * P, 1],
                                                    part[:, tile - 1, :], start=False, stop=False,
                                                    skip_group_check=True)
                            if whole and b < NB - 1:
                                last.then_inc(bank_summed, 1)
                    last.then_inc(x_multiplied, 1)

            pe.wait_ge(constants, 1)
            for n, (t, _) in enumerate(ORDER):
                for b in range(NB):
                    if n:
                        pe.wait_ge(odd_copied if b % 2 else even_copied,
                                   NB // 2 * (n - 1) + b // 2 + 1)
                    nc.tensor.matmul(sums[:, b, PD:PD + 1], zeros[:, :], zeros[:, 0:1],
                                     start=True, stop=True, skip_group_check=True)
                run_head(pe, tables[t], multiply)
                run_rest(pe, tables[t], multiply)

            pe.wait_ge(constants, 2)
            pe.wait_ge(last_q_copied, 1)
            pe.wait_ge(last_emb, 2)
            pe.wait_ge(odd_ready, 1)
            nc.tensor.matmul(sums[0:1, NB - 1, PD:PD + 1], odd_total[:, :], ones[:, :], start=True,
                             stop=True, skip_group_check=True).then_inc(odd_summed, 1)
            pe.wait_ge(flag_ready, 1)
            odd = pe.value_load(odd_flag[0:1, 0:1], min_val=0, max_val=P * NCHUNKS * CHUNK * BATCH)
            with pe.If(odd != 0):
                w_tile, wq_tile = w_rest[:, 0, :], w_square[:, 0, :]
                for t in range(NT):
                    base = sum(TILES[:t])
                    with pe.Fori(0, TILES[t]) as i:
                        pe.wait_ge(gx_landed, 16 * (base + i + 1))
                        pe.wait_ge(gw_landed, 16 * (base + i + 1))
                        pe.wait_ge(gx_ready, 2 * (base + i + 1))
                        for b in range(NB):
                            nc.tensor.matmul(sums[:, b, 0:D], x_ring[0][:, b * P:(b + 1) * P],
                                             w_tile, start=True, stop=True, skip_group_check=True)
                            last = nc.tensor.matmul(sums[:, b, D:2 * D], x_ring[1][:, b * P:(b + 1) * P],
                                                    wq_tile, start=False, stop=True,
                                                    skip_group_check=True)
                        last.then_inc(g_multiplied, 1)

        @block.vector
        def _(dve):
            nc.vector.memset(zeros[:, :], 0.0).then_inc(constants, 1)
            nc.vector.memset(ones[:, :], 1.0).then_inc(constants, 1)
            nc.vector.memset(emb_sum[:, :, :], 0.0).then_inc(constants, 1)
            nc.vector.memset(q_total[:, :, :], 0.0).then_inc(constants, 1)

            def check(group, i, k, g):
                for c, n in enumerate(group.sizes):
                    slot = (group.chunk + c) % SLOTS
                    dve.wait_ge(x_landed[slot], 16 * ((group.chunk + c) // SLOTS + 1 + i))
                    if group.chunk + c >= 2:
                        dve.wait_ge(x_checked, k + c - 1)
                    x = x_ring[slot][:, 0:n * BATCH]
                    nc.vector.scalar_tensor_tensor(out=differs[(group.chunk + c) % 2][:, 0:n * BATCH], in0=x, scalar=0.0,
                                                   in1=x, op0=ALU.is_gt, op1=ALU.not_equal,
                                                   accum_out=odd_counts[:, bass.ds(k + c, 1)]
                                                   ).then_inc(x_checked, 1)

            chain = [0]

            def link(ins, done):
                ins.then_inc(done, 1)
                chain[0] += 1
                dve.wait_ge(done, chain[0])

            def to_stage(n):
                if n >= 2:
                    dve.wait_ge(q_added, n - 1)
                for b in range(1, NB, 2):
                    wait_whole(dve, n, b)
                    nc.vector.tensor_copy(stages[n % 2][:, b, :], sums[:, b, 0:PD]
                                          ).then_inc(odd_copied, 1)

            def combine(n):
                t = ORDER[n][0]
                emb, stage = out_sb[:, t + 1, :, :], stages[n % 2]
                if n == 0:
                    dve.wait_ge(constants, 4)
                dve.wait_ge(even_copied, NB // 2 * (n + 1))
                dve.wait_ge(odd_copied, NB // 2 * (n + 1))
                link(nc.vector.tensor_tensor(low_sum[:, :, :], stage[:, :, D:2 * D],
                                             stage[:, :, 2 * D:3 * D], ALU.add), combined)
                link(nc.vector.tensor_tensor(emb, low_sum[:, :, :], stage[:, :, 0:D], ALU.add),
                     combined)
                nc.vector.tensor_tensor(emb_sum[:, :, :], emb_sum[:, :, :], emb, ALU.add
                                        ).then_inc(emb_added, 1)
                dve.wait_ge(emb_added, n + 1)

            waiting = []
            for n, (t, _) in enumerate(ORDER):
                run_head(dve, tables[t], check)
                run_rest(dve, tables[t], check)
                if n < NT - 1:
                    to_stage(n)
                    waiting.append(n)
                    if TILES[ORDER[n + 1][0]] > 2 or len(waiting) == 2:
                        while waiting:
                            combine(waiting.pop(0))

            dve.wait_ge(x_checked, NCHUNKS)
            nc.vector.tensor_reduce(odd_total[:, :], odd_counts[:, :], mybir.AxisListType.X,
                                    ALU.add).then_inc(odd_ready, 1)

            emb = out_sb[:, ORDER[-1][0] + 1, :, :]

            def over_parts(banks):
                nc.vector.tensor_reduce(
                    emb[:, banks, :], sums[:, banks, 0:3 * D].rearrange("p b (k d) -> p b d k", k=3),
                    mybir.AxisListType.X, ALU.add).then_inc(last_emb, 1)

            wait_whole(dve, NT - 1, NB // 2 - 1)
            over_parts(lower)
            dve.wait_ge(last_q_copied, 1)
            over_parts(upper)
            dve.wait_ge(last_emb, 2)
            fm = out_sb[:, 0, :, :]
            link(nc.vector.tensor_tensor(emb_sum[:, :, :], emb_sum[:, :, :], emb, ALU.add), combined)
            link(nc.vector.scalar_tensor_tensor(out=fm, in0=emb_sum[:, :, :], scalar=0.5,
                                                in1=emb_sum[:, :, :], op0=ALU.mult, op1=ALU.mult),
                 combined)
            dve.wait_ge(last_q_summed, 2)
            link(nc.vector.tensor_tensor(q_total[:, :, :], q_total[:, :, :], q_last[:, :, :],
                                         ALU.add), combined)
            nc.vector.scalar_tensor_tensor(out=fm, in0=q_total[:, :, :], scalar=-0.5, in1=fm,
                                           op0=ALU.mult, op1=ALU.add).then_inc(fm_ready, 1)
            dve.wait_ge(flag_ready, 1)
            odd = dve.value_load(odd_flag[0:1, 0:1], min_val=0, max_val=P * NCHUNKS * CHUNK * BATCH)
            with dve.If(odd != 0):
                steps = [0]

                def g_link(ins):
                    ins.then_inc(g_chain, 1)
                    steps[0] += 1
                    dve.wait_ge(g_chain, steps[0])

                q = q_total[:, :, :]
                dve.wait_ge(stored, 16 * (NT + 1))
                dve.wait_ge(x_multiplied, NCHUNKS)
                dve.wait_ge(parts_ready, NGROUPS)
                nc.vector.nop().then_inc(g_multiplied, 1)
                g_link(nc.vector.memset(q, 0.0))
                g_link(nc.vector.memset(emb_sum[:, :, :], 0.0))
                for t in range(NT):
                    base = sum(TILES[:t])
                    emb = out_sb[:, t + 1, :, :]
                    g_link(nc.vector.memset(emb, 0.0))
                    with dve.Fori(0, TILES[t]) as i:
                        dve.wait_ge(gx_landed, 16 * (base + i + 1))
                        dve.wait_ge(gw_landed, 16 * (base + i + 1))
                        w = w_rest[:, 0, :]
                        nc.vector.tensor_tensor(x_ring[1][:, 0:BATCH], x_ring[0][:, 0:BATCH],
                                                x_ring[0][:, 0:BATCH], ALU.mult).then_inc(gx_ready, 1)
                        nc.vector.tensor_tensor(w_square[:, 0, :], w, w, ALU.mult).then_inc(gx_ready, 1)
                        dve.wait_ge(g_multiplied, base + i + 2)
                        nc.vector.tensor_tensor(emb, emb, sums[:, :, 0:D], ALU.add)
                        nc.vector.tensor_tensor(q, q, sums[:, :, D:2 * D], ALU.add).then_inc(g_added, 1)
                        dve.wait_ge(g_added, base + i + 1)
                    g_link(nc.vector.tensor_tensor(emb_sum[:, :, :], emb_sum[:, :, :], emb, ALU.add))
                g_link(nc.vector.tensor_tensor(fm, emb_sum[:, :, :], emb_sum[:, :, :], ALU.mult))
                g_link(nc.vector.tensor_tensor(fm, fm, q, ALU.subtract))
                nc.vector.tensor_scalar(fm, fm, 0.5, None, ALU.mult).then_inc(g_done, 1)


def kernel(**inputs):
    import numpy as _np
    import concourse.bacc as _bacc
    from concourse.bass_utils import run_bass_kernel_spmd as _run

    nc = _bacc.Bacc("TRN2", target_bir_lowering=False, num_devices=1)
    arrays, xs, ws = {}, [], []
    for i, tiles in enumerate(TILES):
        x, w = _np.asarray(inputs[f"r_x{i}"]), _np.asarray(inputs[f"L0_rec_w{i}"])
        pad = ((0, tiles * P - VOCABS[i]), (0, 0))
        for name, a, aps in ((f"in_x{i}_dram", x.T, xs), (f"in_w{i}_dram", w, ws)):
            a = _np.ascontiguousarray(_np.pad(a, pad))
            arrays[name] = a
            aps.append(nc.dram_tensor(name, a.shape, F32, kind="ExternalInput").ap())
    out = nc.dram_tensor("out_0_dram", (NT + 1, P, NB, D), F32, kind="ExternalOutput").ap()
    rec_kernel(nc, xs, ws, out)
    r = _run(nc, [arrays], core_ids=[0])
    got = r.results[0]["out_0_dram"]
    return _np.ascontiguousarray(got.transpose(2, 1, 0, 3).reshape(BATCH, (NT + 1) * D))
```

```python
from contextlib import ExitStack

import concourse.bass as bass
from concourse import mybir

ALU = mybir.AluOpType
ACT = mybir.ActivationFunctionType
F32 = mybir.dt.float32
BF16 = mybir.dt.bfloat16
I32 = mybir.dt.int32

P = 128
D = 64
BATCH = 1024
NB = BATCH // P
PARTS = 6
PD = PARTS * D
VOCABS = [12500, 6250, 2500, 1250, 625, 250, 1000, 500, 200, 100]
NT = len(VOCABS)
TILES = [-(-v // P) for v in VOCABS]
TAIL = [-(-(v - P * (tiles - 1)) // 16) * 16 for v, tiles in zip(VOCABS, TILES)]

FULL = [2, 2, 2, 2]
ROUNDS = [
    [(8, [[1, 1]]), (6, [[2, 2, 2, 1, 1]]), (4, [[2, 2, 1]]), (9, [[1]]), (5, [[1, 1]])],
    [(3, [[2, 2, 2], [2, 1, 1]])],
    [(2, [FULL, [2, 2, 2], [2, 2, 1, 1]])],
    [(1, [FULL] * 6 + [[1]])],
    [(0, [FULL] * 12 + [[1, 1]])],
    [(7, [[2, 1, 1]])],
]
ORDER = [table for tables in ROUNDS for table in tables]
MERGED = (0, len(ROUNDS) - 1)
LAST = ORDER[-1][0]
FIRSTS = len(ROUNDS[0])
Q_PLACE = FIRSTS + 1
PLACE = {t: n + 1 + (n >= FIRSTS) for n, (t, _) in enumerate(ORDER)}
UNCHECKED = 1
SLOTS = 2 * len(FULL)
CHUNK = max(FULL)
GROUP = sum(FULL)
NGROUPS = sum(len(groups) for _, groups in ORDER)
NCHUNKS = sum(len(g) for _, groups in ORDER for g in groups)


class Group:

    def __init__(self, table, chunk, tile, sizes):
        self.table, self.chunk, self.tile, self.sizes = table, chunk, tile, sizes
        self.tiles = sum(sizes)
        self.rows = P
        self.begins = None
        self.last = False
        self.split = self.next = self.buffer = self.free_after = None
        self.uses = 0


class Table:

    def __init__(self, table, sizes, chunk):
        self.table, self.groups, tile = table, [], 0
        for s in sizes:
            self.groups.append(Group(table, chunk, tile, s))
            chunk, tile = chunk + len(s), tile + sum(s)
        assert tile == TILES[table] and sizes[-1][-1] == 1
        self.groups[-1].rows = TAIL[table]
        self.end = chunk
        pairs = (sizes.count(FULL) - 2) // 2
        self.pairs = pairs if pairs > 1 else 0
        assert all(s == FULL for s in sizes[:2 + 2 * self.pairs]) or not self.pairs
        self.looped = self.groups[1:3] if self.pairs else []
        self.straight = self.groups[1 + 2 * self.pairs:]


def plan():
    tables, chunk = {}, 0
    for t, sizes in ORDER:
        tables[t] = Table(t, sizes, chunk)
        chunk = tables[t].end
    for n, one in enumerate(ROUNDS):
        tables[one[0][0]].groups[0].begins = n
        tables[one[-1][0]].groups[-1].last = True
    flat = [group for t, _ in ORDER for group in tables[t].groups]
    shared = []
    for split, group in enumerate(flat):
        group.split = split
        group.next = flat[split + 1] if split + 1 < len(flat) else None
        if len(tables[group.table].groups) == 1:
            group.buffer = f"of_{group.table}"
            continue
        group.buffer, group.uses = str(len(shared) % 2), len(shared) // 2
        if group in tables[group.table].looped:
            group.free_after = group.chunk - len(group.sizes)
        elif len(shared) >= 2:
            group.free_after = shared[-2].chunk + len(shared[-2].sizes)
        shared.append(group)
    return tables


def rec_kernel(nc, xs, ws, out):
    tables = plan()
    x_dram = [x[0:P * (n - 1)].rearrange("(p t) b -> p (t b)", p=P) if n > 1 else None
              for n, x in zip(TILES, xs)]
    x_tail = [x[P * (n - 1):P * (n - 1) + rows] for n, rows, x in zip(TILES, TAIL, xs)]
    w_dram = [w.rearrange("(p t) d -> p (t d)", p=P) for w in ws]

    with ExitStack() as ctx:
        def sb(name, shape, dt):
            return ctx.enter_context(nc.sbuf_tensor(name, shape, dt))

        def sem(name):
            return ctx.enter_context(nc.semaphore(name))

        sums = ctx.enter_context(nc.psum_tensor("sums", [P, NB, 512], F32))

        x_ring = sb("x_ring", [P, SLOTS * CHUNK * BATCH], F32)
        room = {str(i): GROUP for i in range(2)}
        room.update((table.groups[0].buffer, TILES[t]) for t, table in tables.items()
                    if len(table.groups) == 1)
        parts = {name: sb(f"parts{name}", [P, n, PD], BF16) for name, n in room.items()}
        whole = {name: sb(f"whole{name}", [P, 2, n, D], F32) for name, n in room.items()}
        rest = sb("rest", [P, 2, GROUP, D], F32)
        differs = [sb(f"differs{i}", [P, CHUNK * BATCH], mybir.dt.uint8) for i in range(2)]
        odd_counts = sb("odd_counts", [P, NCHUNKS], F32)
        odd_total = sb("odd_total", [P, 1], F32)
        odd_flag = sb("odd_flag", [1, 1], I32)
        ones = sb("ones", [P, 1], F32)
        zeros = sb("zeros", [P, P], BF16)
        stages = [sb(f"stage{i}", [P, NB, PD], F32) for i in range(2)]
        low_sum = sb("low_sum", [P, NB, D], F32)
        q_low = sb("q_low", [P, NB, D], F32)
        q_round = sb("q_round", [P, NB, D], F32)
        emb_sum = sb("emb_sum", [P, NB, D], F32)
        results = sb("results", [P, NT + 2, NB, D], F32)
        q_total = results[:, Q_PLACE, :, :]

        w_landed = {name: sem(f"w_landed{name}") for name in room}
        x_landed = [sem(f"x_landed{s}") for s in range(SLOTS)]
        x_multiplied = sem("x_multiplied")
        x_checked = sem("x_checked")
        squared = sem("squared")
        high_ready = sem("high_ready")
        rested = sem("rested")
        middle_ready = sem("middle_ready")
        parts_ready = sem("parts_ready")
        constants = sem("constants")
        bank_summed = sem("bank_summed")
        bank_copied = sem("bank_copied")
        combined = sem("combined")
        q_combined = sem("q_combined")
        added = sem("added")
        q_added = sem("q_added")
        half_read = sem("half_read")
        fm_ready = sem("fm_ready")
        last_emb = sem("last_emb")
        odd_ready = sem("odd_ready")
        odd_summed = sem("odd_summed")
        flag_ready = sem("flag_ready")
        stored = sem("stored")

        gx_landed = sem("gx_landed")
        gw_landed = sem("gw_landed")
        gx_ready = sem("gx_ready")
        g_multiplied = sem("g_multiplied")
        g_added = sem("g_added")
        g_chain = sem("g_chain")
        g_done = sem("g_done")

        block = ctx.enter_context(nc.Block())

        lower, upper = slice(0, NB // 2), slice(NB // 2, NB)

        def run_head(eng, table, step):
            group = table.groups[0]
            step(group, 0, group.chunk, group.split)

        def run_rest(eng, table, step):
            if table.pairs:
                with eng.Fori(0, table.pairs) as i:
                    for group in table.looped:
                        step(group, i, group.chunk + SLOTS * i, group.split + 2 * i)
            for group in table.straight:
                step(group, 0, group.chunk, group.split)

        def in_slot(slot, elements):
            at = slot * CHUNK * BATCH
            return x_ring[:, at:at + elements]

        def is_tail(group, c):
            return group is tables[group.table].groups[-1] and c == len(group.sizes) - 1

        def rows_of(group, c):
            return group.rows if is_tail(group, c) else P

        def part_of(group, kind):
            return parts[group.buffer][:, 0:group.tiles, :].rearrange(
                "p t (m k d) -> p m k t d", m=2, k=3)[:, :, kind]

        def wait_whole(eng, n, b):
            if b < NB - 1:
                eng.wait_ge(bank_summed, (NB - 1) * n + b + 1)
            else:
                eng.wait_ge(x_multiplied, tables[ROUNDS[n][-1][0]].end)

        @block.sync
        def _(sp):
            def load_w(group, i, g):
                if group.uses:
                    sp.wait_ge(rested, g - 1)
                at = (group.tile + 2 * group.tiles * i) * D
                sp.dma_start(whole[group.buffer][:, 0, 0:group.tiles, :],
                             w_dram[group.table][:, bass.ds(at, group.tiles * D)]
                             ).then_inc(w_landed[group.buffer], 16)

            def load(group, i, k, g):
                at = group.tile + 2 * group.tiles * i
                for c, n in enumerate(group.sizes):
                    slot = (group.chunk + c) % SLOTS
                    if group.chunk + c >= SLOTS:
                        sp.wait_ge(x_multiplied, k + (c + 1 - SLOTS))
                        sp.wait_ge(x_checked, k + (c + 1 - SLOTS))
                    rows = rows_of(group, c)
                    sp.dma_start(in_slot(slot, n * BATCH)[0:rows],
                                 x_dram[group.table][:, bass.ds(at * BATCH, n * BATCH)]
                                 if not is_tail(group, c) else x_tail[group.table]
                                 ).then_inc(x_landed[slot], 16)
                    at = at + n
                    if c == 0:
                        if not group.split:
                            load_w(group, i, g)
                        if group.next:
                            load_w(group.next, i, g + 1)

            for t, _ in ORDER:
                run_head(sp, tables[t], load)
                run_rest(sp, tables[t], load)
            for n, one in enumerate(ROUNDS[:-1]):
                sp.wait_ge(added, n + 1)
                for t, _ in one:
                    sp.dma_start(out[t + 1], results[:, PLACE[t], :, :]).then_inc(stored, 16)
            sp.wait_ge(fm_ready, 1)
            sp.dma_start(out[0], results[:, 0, :, :]).then_inc(stored, 16)
            sp.wait_ge(flag_ready, 1)
            odd = sp.value_load(odd_flag[0:1, 0:1], min_val=0, max_val=P * NCHUNKS * CHUNK * BATCH)
            sp.wait_ge(stored, 16 * (NT + 1))
            with sp.If(odd != 0):
                for t in range(NT):
                    base = sum(TILES[:t])

                    def load_tile(i, rows, x):
                        sp.wait_ge(g_multiplied, base + i + 1)
                        sp.dma_start(in_slot(0, BATCH)[0:rows], x).then_inc(gx_landed, 16)
                        sp.dma_start(rest[:, 0, 0, :], w_dram[t][:, bass.ds(i * D, D)]
                                     ).then_inc(gw_landed, 16)

                    if TILES[t] > 1:
                        with sp.Fori(0, TILES[t] - 1) as i:
                            load_tile(i, P, x_dram[t][:, bass.ds(i * BATCH, BATCH)])
                    load_tile(TILES[t] - 1, TAIL[t], x_tail[t])
                sp.wait_ge(g_done, 1)
                sp.dma_start(out[0], results[:, 0, :, :]).then_inc(stored, 16)
                for t in range(NT):
                    sp.dma_start(out[t + 1], results[:, PLACE[t], :, :]).then_inc(stored, 16)
                sp.wait_ge(stored, 2 * 16 * (NT + 1))

        @block.scalar
        def _(act):
            def split(group, i, k, g):
                both = whole[group.buffer][:, :, 0:group.tiles, :]
                act.wait_ge(w_landed[group.buffer], 16 * (group.uses + 1 + i))
                nc.scalar.activation(both[:, 1], both[:, 0], ACT.Square).then_inc(squared, 1)
                if group.free_after is not None:
                    act.wait_ge(x_multiplied, k - (group.chunk - group.free_after))
                act.wait_ge(squared, g + 1)
                nc.scalar.activation(part_of(group, 0), both, ACT.Copy).then_inc(high_ready, 1)
                act.wait_ge(rested, g + 1)
                nc.scalar.activation(part_of(group, 1), rest[:, :, 0:group.tiles, :], ACT.Copy
                                     ).then_inc(middle_ready, 1)

            def copy_out(n):
                if n >= 3:
                    act.wait_ge(added, n - 1)
                    act.wait_ge(q_added, n - 2)
                for b in range(NB):
                    wait_whole(act, n, b)
                    if n == 0:
                        bank = sums[:, b, 0:(FIRSTS + 1) * D].rearrange("p (r d) -> p r d", d=D)
                        nc.scalar.activation(results[:, 1:Q_PLACE + 1, b, :], bank, ACT.Copy
                                             ).then_inc(bank_copied, 1)
                    else:
                        nc.scalar.activation(stages[n % 2][:, b, :], sums[:, b, 0:PD], ACT.Copy
                                             ).then_inc(bank_copied, 1)

            for n, one in enumerate(ROUNDS):
                for t, _ in one:
                    run_head(act, tables[t], split)
                    if n and t == one[0][0]:
                        copy_out(n - 1)
                    run_rest(act, tables[t], split)

            for step, banks in enumerate((lower, upper)):
                act.wait_ge(half_read, step + 1)
                nc.scalar.activation(results[:, PLACE[LAST], banks, :], sums[:, banks, 0:D], ACT.Copy
                                     ).then_inc(last_emb, 1)
            act.wait_ge(last_emb, 2)
            act.dma_start(out[LAST + 1], results[:, PLACE[LAST], :, :]).then_inc(stored, 16)
            act.wait_ge(odd_summed, 1)
            nc.scalar.activation(odd_flag[0:1, 0:1], sums[0:1, NB - 1, 0:1], ACT.Copy
                                 ).then_inc(flag_ready, 1)

        @block.gpsimd
        def _(pool):
            for n in range(1, len(ROUNDS) - 1):
                stage = stages[n % 2]
                pool.wait_ge(bank_copied, NB * (n + 1))
                nc.gpsimd.tensor_tensor(q_low[:, :, :], stage[:, :, 4 * D:5 * D],
                                        stage[:, :, 5 * D:], ALU.add).then_inc(q_combined, 1)
                pool.wait_ge(q_combined, 2 * n - 1)
                nc.gpsimd.tensor_tensor(q_round[:, :, :], q_low[:, :, :], stage[:, :, 3 * D:4 * D],
                                        ALU.add).then_inc(q_combined, 1)
                pool.wait_ge(q_combined, 2 * n)
                nc.gpsimd.tensor_tensor(q_total, q_total, q_round[:, :, :], ALU.add
                                        ).then_inc(q_added, 1)
                pool.wait_ge(q_added, n)

        @block.tensor
        def _(pe):
            def products(bank, x, w, places):
                if places is None:
                    return nc.tensor.matmul(sums[:, bank, 0:PD], x, w, start=False, stop=False,
                                            skip_group_check=True)
                at, q_at = places
                columns = sums[:, bank, :].rearrange("p (r d) -> p r d", d=D)
                for part in (2, 1, 0):
                    last = nc.tensor.matmul(
                        columns[:, at:q_at + 1:q_at - at, :], x,
                        w.rearrange("p (m k d) -> p k m d", m=2, k=3)[:, part], start=False,
                        stop=False, skip_group_check=True)
                return last

            places = {t: (n, len(ROUNDS[r])) for r in MERGED for n, (t, _) in enumerate(ROUNDS[r])}

            def clear(n, b):
                if n:
                    pe.wait_ge(bank_copied, NB * (n - 1) + b + 1)
                nc.tensor.matmul(sums[:, b, PD:PD + 1], zeros[:, :], zeros[:, 0:1],
                                 start=True, stop=True, skip_group_check=True)

            def multiply(group, i, k, g):
                part = parts[group.buffer]
                pe.wait_ge(parts_ready, g + 1)
                tile = 0
                for c, n in enumerate(group.sizes):
                    slot = (group.chunk + c) % SLOTS
                    pe.wait_ge(x_landed[slot], 16 * ((group.chunk + c) // SLOTS + 1 + i))
                    x = in_slot(slot, CHUNK * BATCH).bitcast(BF16).rearrange(
                        "p (t b h) -> p t b h", h=2, b=BATCH)
                    rows = rows_of(group, c)
                    for b in range(NB):
                        if group.begins is not None and c == 0:
                            clear(group.begins, b)
                        for t in range(n):
                            last = products(b, x[0:rows, t, b * P:(b + 1) * P, 1],
                                            part[0:rows, tile + t, :],
                                            places.get(group.table))
                        if group.last and c == len(group.sizes) - 1 and b < NB - 1:
                            last.then_inc(bank_summed, 1)
                    tile += n
                    last.then_inc(x_multiplied, 1)

            pe.wait_ge(constants, 1)
            for t, _ in ORDER:
                run_head(pe, tables[t], multiply)
                run_rest(pe, tables[t], multiply)

            pe.wait_ge(constants, 2)
            pe.wait_ge(last_emb, 2)
            pe.wait_ge(odd_ready, 1)
            nc.tensor.matmul(sums[0:1, NB - 1, 0:1], odd_total[:, :], ones[:, :], start=True,
                             stop=True, skip_group_check=True).then_inc(odd_summed, 1)
            pe.wait_ge(flag_ready, 1)
            odd = pe.value_load(odd_flag[0:1, 0:1], min_val=0, max_val=P * NCHUNKS * CHUNK * BATCH)
            with pe.If(odd != 0):
                w_tile, wq_tile = rest[:, 0, 0, :], rest[:, 1, 0, :]
                for t in range(NT):
                    base = sum(TILES[:t])

                    def multiply_tile(i, rows):
                        pe.wait_ge(gx_landed, 16 * (base + i + 1))
                        pe.wait_ge(gw_landed, 16 * (base + i + 1))
                        pe.wait_ge(gx_ready, 2 * (base + i + 1))
                        for b in range(NB):
                            block_b = slice(b * P, (b + 1) * P)
                            nc.tensor.matmul(sums[:, b, 0:D], in_slot(0, BATCH)[0:rows, block_b],
                                             w_tile[0:rows], start=True, stop=True,
                                             skip_group_check=True)
                            last = nc.tensor.matmul(sums[:, b, D:2 * D],
                                                    in_slot(1, BATCH)[0:rows, block_b],
                                                    wq_tile[0:rows], start=False, stop=True,
                                                    skip_group_check=True)
                        last.then_inc(g_multiplied, 1)

                    if TILES[t] > 1:
                        with pe.Fori(0, TILES[t] - 1) as i:
                            multiply_tile(i, P)
                    multiply_tile(TILES[t] - 1, TAIL[t])

        @block.vector
        def _(dve):
            nc.vector.memset(zeros[:, :], 0.0).then_inc(constants, 1)
            nc.vector.memset(ones[:, :], 1.0).then_inc(constants, 1)
            nc.vector.memset(odd_counts[:, :], 0.0).then_inc(constants, 1)
            dve.wait_ge(constants, 3)

            def check_chunk(group, i, k, c):
                n, slot = group.sizes[c], (group.chunk + c) % SLOTS
                dve.wait_ge(x_landed[slot], 16 * ((group.chunk + c) // SLOTS + 1 + i))
                if group.chunk + c >= 2:
                    dve.wait_ge(x_checked, k + c - 1)
                rows = rows_of(group, c)
                x = in_slot(slot, n * BATCH)[0:rows]
                nc.vector.scalar_tensor_tensor(out=differs[(group.chunk + c) % 2][0:rows, 0:n * BATCH],
                                               in0=x, scalar=0.0, in1=x, op0=ALU.is_gt,
                                               op1=ALU.not_equal,
                                               accum_out=odd_counts[0:rows, bass.ds(k + c, 1)]
                                               ).then_inc(x_checked, 1)

            def subtract_high(group, g):
                if group.split:
                    dve.wait_ge(parts_ready, g)
                dve.wait_ge(high_ready, g + 1)
                nc.vector.tensor_tensor(rest[:, :, 0:group.tiles, :],
                                        whole[group.buffer][:, :, 0:group.tiles, :],
                                        part_of(group, 0), ALU.subtract).then_inc(rested, 1)

            def subtract_middle(group, g):
                dve.wait_ge(middle_ready, g + 1)
                nc.vector.tensor_tensor(part_of(group, 2), rest[:, :, 0:group.tiles, :],
                                        part_of(group, 1), ALU.subtract).then_inc(parts_ready, 1)

            def check(group, i, k, g):
                chunks = len(group.sizes)
                high_at = max(chunks - 3, 0)
                middle_at = min(high_at + 1, chunks - 1)
                for c in range(chunks):
                    if group.chunk + c < NCHUNKS - UNCHECKED:
                        check_chunk(group, i, k, c)
                    if group.next and c == high_at:
                        subtract_high(group.next, g + 1)
                    if group.next and c == middle_at:
                        subtract_middle(group.next, g + 1)

            def combine(n):
                dve.wait_ge(bank_copied, NB * (n + 1))
                if n == 0:
                    nc.vector.tensor_reduce(
                        emb_sum[:, :, :],
                        results[:, 1:FIRSTS + 1, :, :].rearrange("p t b d -> p b d t"),
                        mybir.AxisListType.X, ALU.add).then_inc(added, 1)
                    return
                emb, stage = results[:, PLACE[ROUNDS[n][0][0]], :, :], stages[n % 2]
                nc.vector.tensor_tensor(low_sum[:, :, :], stage[:, :, D:2 * D],
                                        stage[:, :, 2 * D:3 * D], ALU.add).then_inc(combined, 1)
                dve.wait_ge(combined, 2 * n - 1)
                nc.vector.tensor_tensor(emb, low_sum[:, :, :], stage[:, :, 0:D], ALU.add
                                        ).then_inc(combined, 1)
                dve.wait_ge(combined, 2 * n)
                nc.vector.tensor_tensor(emb_sum[:, :, :], emb_sum[:, :, :], emb, ALU.add
                                        ).then_inc(added, 1)

            subtract_high(tables[ORDER[0][0]].groups[0], 0)
            subtract_middle(tables[ORDER[0][0]].groups[0], 0)
            for n, one in enumerate(ROUNDS):
                for t, _ in one:
                    run_head(dve, tables[t], check)
                    if n and t == one[0][0]:
                        combine(n - 1)
                    run_rest(dve, tables[t], check)
            dve.wait_ge(added, len(ROUNDS) - 1)
            dve.wait_ge(q_added, len(ROUNDS) - 2)

            for banks in (lower, upper):
                wait_whole(dve, len(ROUNDS) - 1, banks.stop - 1)
                nc.vector.tensor_tensor(emb_sum[:, banks, :], sums[:, banks, 0:D],
                                        emb_sum[:, banks, :], ALU.add)
                nc.vector.tensor_tensor(q_total[:, banks, :], sums[:, banks, D:2 * D],
                                        q_total[:, banks, :], ALU.add).then_inc(half_read, 1)
            dve.wait_ge(half_read, 2)
            fm = results[:, 0, :, :]
            nc.vector.scalar_tensor_tensor(out=fm, in0=emb_sum[:, :, :], scalar=0.5,
                                           in1=emb_sum[:, :, :], op0=ALU.mult, op1=ALU.mult
                                           ).then_inc(combined, 1)
            dve.wait_ge(combined, 2 * (len(ROUNDS) - 2) + 1)
            nc.vector.scalar_tensor_tensor(out=fm, in0=q_total, scalar=-0.5, in1=fm,
                                           op0=ALU.mult, op1=ALU.add).then_inc(fm_ready, 1)

            final = tables[LAST].groups[-1]
            for c in range(len(final.sizes) - UNCHECKED, len(final.sizes)):
                check_chunk(final, 0, final.chunk, c)
            dve.wait_ge(x_checked, NCHUNKS)
            nc.vector.tensor_reduce(odd_total[:, :], odd_counts[:, :], mybir.AxisListType.X,
                                    ALU.add).then_inc(odd_ready, 1)
            dve.wait_ge(flag_ready, 1)
            odd = dve.value_load(odd_flag[0:1, 0:1], min_val=0, max_val=P * NCHUNKS * CHUNK * BATCH)
            with dve.If(odd != 0):
                steps = [0]

                def g_link(ins):
                    ins.then_inc(g_chain, 1)
                    steps[0] += 1
                    dve.wait_ge(g_chain, steps[0])

                q = q_total
                dve.wait_ge(stored, 16 * (NT + 1))
                dve.wait_ge(x_multiplied, NCHUNKS)
                dve.wait_ge(parts_ready, NGROUPS)
                nc.vector.nop().then_inc(g_multiplied, 1)
                g_link(nc.vector.memset(q, 0.0))
                g_link(nc.vector.memset(emb_sum[:, :, :], 0.0))
                for t in range(NT):
                    base = sum(TILES[:t])
                    emb = results[:, PLACE[t], :, :]
                    g_link(nc.vector.memset(emb, 0.0))

                    def add_tile(i, rows):
                        dve.wait_ge(gx_landed, 16 * (base + i + 1))
                        dve.wait_ge(gw_landed, 16 * (base + i + 1))
                        x, w = in_slot(0, BATCH)[0:rows], rest[:, 0, 0, :]
                        nc.vector.tensor_tensor(in_slot(1, BATCH)[0:rows], x, x, ALU.mult
                                                ).then_inc(gx_ready, 1)
                        nc.vector.tensor_tensor(rest[:, 1, 0, :], w, w, ALU.mult).then_inc(gx_ready, 1)
                        dve.wait_ge(g_multiplied, base + i + 2)
                        nc.vector.tensor_tensor(emb, emb, sums[:, :, 0:D], ALU.add)
                        nc.vector.tensor_tensor(q, q, sums[:, :, D:2 * D], ALU.add).then_inc(g_added, 1)
                        dve.wait_ge(g_added, base + i + 1)

                    if TILES[t] > 1:
                        with dve.Fori(0, TILES[t] - 1) as i:
                            add_tile(i, P)
                    add_tile(TILES[t] - 1, TAIL[t])
                    g_link(nc.vector.tensor_tensor(emb_sum[:, :, :], emb_sum[:, :, :], emb, ALU.add))
                g_link(nc.vector.tensor_tensor(fm, emb_sum[:, :, :], emb_sum[:, :, :], ALU.mult))
                g_link(nc.vector.tensor_tensor(fm, fm, q, ALU.subtract))
                nc.vector.tensor_scalar(fm, fm, 0.5, None, ALU.mult).then_inc(g_done, 1)


def kernel(**inputs):
    import numpy as _np
    import concourse.bacc as _bacc
    from concourse.bass_utils import run_bass_kernel_spmd as _run

    nc = _bacc.Bacc("TRN2", target_bir_lowering=False, num_devices=1)
    arrays, xs, ws = {}, [], []
    for i, (tiles, rows) in enumerate(zip(TILES, TAIL)):
        x, w = _np.asarray(inputs[f"r_x{i}"]), _np.asarray(inputs[f"L0_rec_w{i}"])
        full = P * (tiles - 1)
        x = _np.pad(x.T, ((0, full + rows - VOCABS[i]), (0, 0)))
        w = _np.pad(w, ((0, full + P - VOCABS[i]), (0, 0)))
        w = _np.concatenate([w[:full].reshape(P, tiles - 1, D), w[full:].reshape(P, 1, D)], 1)
        for name, a, aps in ((f"in_x{i}_dram", x, xs), (f"in_w{i}_dram", w.reshape(P * tiles, D), ws)):
            a = _np.ascontiguousarray(a)
            arrays[name] = a
            aps.append(nc.dram_tensor(name, a.shape, F32, kind="ExternalInput").ap())
    out = nc.dram_tensor("out_0_dram", (NT + 1, P, NB, D), F32, kind="ExternalOutput").ap()
    rec_kernel(nc, xs, ws, out)
    r = _run(nc, [arrays], core_ids=[0])
    got = r.results[0]["out_0_dram"]
    return _np.ascontiguousarray(got.transpose(2, 1, 0, 3).reshape(BATCH, (NT + 1) * D))
```
